# Optimizing a Trainium2 kernel written in Bass

```python
import numpy as np
import jax
import jax.numpy as jnp

def _softmax(x, axis=-1):
    return jax.nn.softmax(x, axis=axis)

def _gelu(x):
    return jax.nn.gelu(x, approximate=True)

def _silu(x):
    return jax.nn.silu(x)

def _sigmoid(x):
    return jax.nn.sigmoid(x)

def _layernorm(x, axis=-1, eps=1e-05):
    m = jnp.mean(x, axis=axis, keepdims=True)
    v = jnp.var(x, axis=axis, keepdims=True)
    return (x - m) / jnp.sqrt(v + eps)

def _scatter_add(tgt, idx, src, axis=0):
    return tgt.at[idx].add(src)

def _segment_sum(src, seg, n):
    return jax.ops.segment_sum(src, seg, n)
kernel_name = 'mk_seq_preln_d2_jaxref_r4_c7875f'

def setup_inputs(seed: int=0):
    np.random.seed(seed)
    _w = jnp.asarray

    def _L0_attn_setup():
        import jax, jax.numpy as jnp
        import numpy as np
        N_HEADS = 16
        key = jax.random.key(seed)
        ks = jax.random.split(key, 5)
        B, S, D = (2, 512, 256)
        dk = D // N_HEADS
        std = float(np.sqrt(2.0 / (D + D)))
        x = jax.random.normal(ks[0], (B, S, D), dtype=jnp.float32)
        w_q = jax.random.normal(ks[1], (D, D), dtype=jnp.float32) * std
        w_k = jax.random.normal(ks[2], (dk, D), dtype=jnp.float32) * std
        w_v = jax.random.normal(ks[3], (dk, D), dtype=jnp.float32) * std
        w_out = jax.random.normal(ks[4], (D, D), dtype=jnp.float32) * std
        softmax_scale = jnp.ones((1,), dtype=jnp.float32) / jnp.sqrt(jnp.float32(dk))
        return {'x': x, 'w_q': w_q, 'w_k': w_k, 'w_v': w_v, 'w_out': w_out, 'softmax_scale': softmax_scale}
    _L0_attn_in = _L0_attn_setup()

    def _L0_ffn_setup():
        import jax, jax.numpy as jnp
        import numpy as np
        FEATURES = 256
        D_IN = 256

        def fp8_gemm_optimized(x, input_scale, kernel, kernel_scale):
            s_in = input_scale[0]
            s_k = kernel_scale[0]
            x_q = (x.astype(jnp.float32) / s_in).astype(jnp.float8_e4m3fn)
            k_q = (kernel.astype(jnp.float32) / s_k).astype(jnp.float8_e4m3fn)
            y = jnp.dot(x_q.astype(jnp.float32), k_q.astype(jnp.float32), preferred_element_type=jnp.float32)
            return y * (s_in * s_k)
        key = jax.random.key(seed)
        kx, kk, kb = jax.random.split(key, 3)
        x = jax.random.normal(kx, (4, 2048, D_IN), dtype=jnp.float32)
        limit = np.sqrt(6.0 / (D_IN + FEATURES)).astype(np.float32)
        kernel = jax.random.uniform(kk, (D_IN, FEATURES), dtype=jnp.float32, minval=-limit, maxval=limit).astype(jnp.bfloat16)
        input_scale = jnp.ones((1,), dtype=jnp.float32)
        kernel_scale = jnp.ones((1,), dtype=jnp.float32)
        bias = jnp.zeros((FEATURES,), dtype=jnp.bfloat16)
        return {'x': x, 'kernel': kernel, 'input_scale': input_scale, 'kernel_scale': kernel_scale, 'bias': bias}
    _L0_ffn_in = _L0_ffn_setup()

    def _L1_attn_setup():
        import jax, jax.numpy as jnp
        import numpy as np
        NUM_HEADS = 16
        N_EMBD = 256

        def alibi_bias(num_heads: int, seq_len: int) -> jnp.ndarray:
            pos = jnp.arange(seq_len, dtype=jnp.float32)
            dgrid = pos[None, :] - pos[:, None]
            slopes = 2.0 ** (-8.0 / num_heads * (jnp.arange(num_heads, dtype=jnp.float32) + 1.0))
            bias = slopes[:, None, None] * dgrid[None, :, :]
            return jnp.where(dgrid[None, :, :] > 0, -jnp.inf, bias)
        key = jax.random.key(seed)
        k1, k2, k3 = jax.random.split(key, 3)
        B, L, E = (2, 512, N_EMBD)
        x = jax.random.normal(k1, (B, L, E), dtype=jnp.float32)
        w_in = jax.random.normal(k2, (3 * E, E), dtype=jnp.float32) * 0.02
        w_out = jax.random.normal(k3, (E, E), dtype=jnp.float32) * 0.02
        return {'x': x, 'w_in': w_in, 'w_out': w_out}
    _L1_attn_in = _L1_attn_setup()

    def _L1_ffn_setup():
        import jax, jax.numpy as jnp
        import numpy as np
        ALPHA = 1.0
        key = jax.random.key(seed)
        ks = jax.random.split(key, 7)
        B, S, IN, OUT = (8, 2048, 256, 256)
        RANK, DDIM, UDIM = (4, 100, 50)
        return {'hidden_states': jax.random.normal(ks[0], (B, S, IN), dtype=jnp.float32), 'W': jax.random.normal(ks[1], (OUT, IN), dtype=jnp.float32) * 0.02, 'b': jax.random.normal(ks[2], (OUT,), dtype=jnp.float32) * 0.02, 'lora_down': jax.random.normal(ks[3], (RANK, DDIM), dtype=jnp.float32) * 0.1, 'lora_up': jax.random.normal(ks[4], (UDIM, RANK), dtype=jnp.float32) * 0.1, 'down_aux': jax.random.normal(ks[5], (DDIM, IN), dtype=jnp.float32) * 0.03, 'up_aux': jax.random.normal(ks[6], (OUT, UDIM), dtype=jnp.float32) * 0.03}
    _L1_ffn_in = _L1_ffn_setup()
    _d = {'L0_attn_x': _L0_attn_in['x'], 'L0_attn_w_q': _L0_attn_in['w_q'], 'L0_attn_w_k': _L0_attn_in['w_k'], 'L0_attn_w_v': _L0_attn_in['w_v'], 'L0_attn_w_out': _L0_attn_in['w_out'], 'L0_attn_softmax_scale': _L0_attn_in['softmax_scale'], 'L0_ffn_kernel': _L0_ffn_in['kernel'], 'L0_ffn_input_scale': _L0_ffn_in['input_scale'], 'L0_ffn_kernel_scale': _L0_ffn_in['kernel_scale'], 'L0_ffn_bias': _L0_ffn_in['bias'], 'L1_attn_w_in': _L1_attn_in['w_in'], 'L1_attn_w_out': _L1_attn_in['w_out'], 'L1_ffn_W': _L1_ffn_in['W'], 'L1_ffn_b': _L1_ffn_in['b'], 'L1_ffn_lora_down': _L1_ffn_in['lora_down'], 'L1_ffn_lora_up': _L1_ffn_in['lora_up'], 'L1_ffn_down_aux': _L1_ffn_in['down_aux'], 'L1_ffn_up_aux': _L1_ffn_in['up_aux']}
    _x0 = _d['L0_attn_x']
    _d['L0_attn_x'] = jax.random.normal(jax.random.fold_in(jax.random.key(seed), 1), (32, 512, 256), dtype=_x0.dtype)
    del _x0
    return _d

def reference(L0_attn_x, L0_attn_w_q, L0_attn_w_k, L0_attn_w_v, L0_attn_w_out, L0_attn_softmax_scale, L0_ffn_kernel, L0_ffn_input_scale, L0_ffn_kernel_scale, L0_ffn_bias, L1_attn_w_in, L1_attn_w_out, L1_ffn_W, L1_ffn_b, L1_ffn_lora_down, L1_ffn_lora_up, L1_ffn_down_aux, L1_ffn_up_aux):

    def _L0_attn_ref(x, w_q, w_k, w_v, w_out, softmax_scale):
        import jax, jax.numpy as jnp
        import numpy as np
        N_HEADS = 16
        B, S, D = x.shape
        dk = D // N_HEADS
        q = (x @ w_q.T).reshape(B, S, N_HEADS, dk)
        k = x @ w_k.T
        v = x @ w_v.T
        scores = jnp.einsum('bshd,btd->bhst', q, k) * softmax_scale[0]
        attn = jax.nn.softmax(scores, axis=-1)
        out = jnp.einsum('bhst,btd->bshd', attn, v).reshape(B, S, D)
        return out @ w_out.T

    def _L0_ffn_ref(x, kernel, input_scale, kernel_scale, bias):
        import jax, jax.numpy as jnp
        import numpy as np
        FEATURES = 256
        D_IN = 256

        def fp8_gemm_optimized(x, input_scale, kernel, kernel_scale):
            s_in = input_scale[0]
            s_k = kernel_scale[0]
            x_q = (x.astype(jnp.float32) / s_in).astype(jnp.float8_e4m3fn)
            k_q = (kernel.astype(jnp.float32) / s_k).astype(jnp.float8_e4m3fn)
            y = jnp.dot(x_q.astype(jnp.float32), k_q.astype(jnp.float32), preferred_element_type=jnp.float32)
            return y * (s_in * s_k)
        dtype = jnp.bfloat16
        x = x.astype(dtype)
        orig_shape = x.shape
        x2 = x.reshape(-1, x.shape[-1])
        y = fp8_gemm_optimized(x2, input_scale, kernel, kernel_scale)
        y = y.astype(dtype) + bias
        return y.reshape(orig_shape[:-1] + (FEATURES,))

    def _L1_attn_ref(x, w_in, w_out):
        import jax, jax.numpy as jnp
        import numpy as np
        NUM_HEADS = 16
        N_EMBD = 256

        def alibi_bias(num_heads: int, seq_len: int) -> jnp.ndarray:
            pos = jnp.arange(seq_len, dtype=jnp.float32)
            dgrid = pos[None, :] - pos[:, None]
            slopes = 2.0 ** (-8.0 / num_heads * (jnp.arange(num_heads, dtype=jnp.float32) + 1.0))
            bias = slopes[:, None, None] * dgrid[None, :, :]
            return jnp.where(dgrid[None, :, :] > 0, -jnp.inf, bias)
        B, L, E = x.shape
        H = NUM_HEADS
        D = E // H
        qkv = jnp.einsum('ble,fe->blf', x, w_in)
        q, k, v = jnp.split(qkv, 3, axis=-1)

        def to_heads(t):
            return t.reshape(B, L, H, D).transpose(0, 2, 1, 3)
        q, k, v = (to_heads(q), to_heads(k), to_heads(v))
        scale = 1.0 / jnp.sqrt(jnp.asarray(D, dtype=x.dtype))
        scores = jnp.einsum('bhqd,bhkd->bhqk', q, k) * scale
        scores = scores + alibi_bias(H, L)[None]
        attn = jax.nn.softmax(scores, axis=-1)
        ctx = jnp.einsum('bhqk,bhkd->bhqd', attn, v)
        ctx = ctx.transpose(0, 2, 1, 3).reshape(B, L, E)
        return jnp.einsum('ble,fe->blf', ctx, w_out)

    def _L1_ffn_ref(hidden_states, W, b, lora_down, lora_up, down_aux, up_aux):
        import jax, jax.numpy as jnp
        import numpy as np
        ALPHA = 1.0
        lilora_weight = up_aux @ (lora_up @ (lora_down @ down_aux))
        base = jnp.einsum('bsi,oi->bso', hidden_states, W) + b
        delta = jnp.einsum('bsi,oi->bso', hidden_states, lilora_weight)
        return base + ALPHA * delta
    x = L0_attn_x
    x = x + _L0_attn_ref(_layernorm(x, axis=-1), L0_attn_w_q, L0_attn_w_k, L0_attn_w_v, L0_attn_w_out, L0_attn_softmax_scale)
    x = x + _L0_ffn_ref(_layernorm(x, axis=-1), L0_ffn_kernel, L0_ffn_input_scale, L0_ffn_kernel_scale, L0_ffn_bias)
    x = x + _L1_attn_ref(_layernorm(x, axis=-1), L1_attn_w_in, L1_attn_w_out)
    x = x + _L1_ffn_ref(_layernorm(x, axis=-1), L1_ffn_W, L1_ffn_b, L1_ffn_lora_down, L1_ffn_lora_up, L1_ffn_down_aux, L1_ffn_up_aux)
    return x

_drawn_inputs = setup_inputs


def setup_inputs(seed=0):
    import zlib

    import numpy as np

    out = dict(_drawn_inputs(seed))
    spreads = {}
    factors = {'L1_attn_w_in': 2.991,
     'L1_attn_w_out': 2.975,
     'L1_ffn_b': 27.15,
     'L1_ffn_lora_down': 4.529,
     'L1_ffn_lora_up': 5.02,
     'L1_ffn_down_aux': 4.702,
     'L1_ffn_up_aux': 4.646}
    for name, (base, spread) in spreads.items():
        noise = np.random.default_rng([zlib.crc32(name.encode()), seed]).standard_normal(out[name].shape)
        drawn = base * np.exp(spread * noise) if base else spread * noise
        out[name] = jnp.asarray(drawn.astype(out[name].dtype))
    for name, factor in factors.items():
        out[name] = (out[name] * factor).astype(out[name].dtype)
    return out
```

```python
from contextlib import ExitStack

import concourse.bass as bass
from concourse import mybir

F32 = mybir.dt.float32
BF16 = mybir.dt.bfloat16
I32 = mybir.dt.int32
ALU = mybir.AluOpType
ACT = mybir.ActivationFunctionType
AX = mybir.AxisListType

P = 128
BANK = 512
EPS = 1e-5
HEADS = 16
DH = 16
QUAD = 4
VW = 32
Q_PARTS = [0, 0, 1, 1, 0, 2]
K_PARTS = [0, 1, 0, 1, 2, 0]
QK_ROWS = DH * len(Q_PARTS)
M_ROWS = 2
FP8_MIN_NORMAL = 2.0 ** -6
FP8_MAGIC = 1.5 * 2.0 ** 20
FP8_OVERFLOW = 1.1 * 2.0 ** 119
EXPONENT_BITS = 0x7F800000
LOWEST = -3.4028235e38

TASKS = {
    0: [
        [("m", 1, 0)], [("otr", 2, -1)], [], [("ft", 0, -2)],
        [("m", 2, 0), ("ffn", 0, -2)], [("otr", 3, -1), ("ffn", 1, -2)], [("ont", 0, -1), ("xt", 0, 2)],
        [("ont", 1, -1), ("v", 0, 1)],
        [("m", 3, 0), ("xt", 1, 2)], [("otr", 0, 0), ("out", 0, -1)], [("out", 1, -1)], [("kv", 0, 2)],
        [("m", 0, 1), ("qk", 0, 2)], [("otr", 1, 0)], [("qk", 1, 2)], [],
    ],
    1: [
        [("m", 1, 0)], [("otr", 2, -1)], [("ft", 0, -2)], [("ft", 1, -2)],
        [("m", 2, 0), ("ffn", 0, -2)], [("otr", 3, -1), ("ffn", 1, -2)], [("v", 0, 1)],
        [("ont", 0, -1), ("v", 1, 1)],
        [("m", 3, 0), ("ont", 1, -1)], [("otr", 0, 0), ("out", 0, -1)], [("out", 1, -1), ("xt", 0, 2)], [("xt", 1, 2)],
        [("m", 0, 1), ("qk", 0, 2)], [("otr", 1, 0), ("qk", 1, 2)], [("qk", 2, 2)], [("qk", 3, 2)],
    ],
}
BANKS = {0: (2, 3), 1: (2, 3)}
ORDER = {0: 'A0 E0 A1 E1 PV A2 E2 A3 E3', 1: 'A0 E0 A1 E1 PV A2 E2 A3 E3'}
PER = {
    0: {"m": 4, "otr": 4, "ont": 2, "out": 2, "xt": 2, "qk": 2, "kv": 1, "v": 1, "ft": 1, "ffn": 2},
    1: {"m": 4, "otr": 4, "ont": 2, "out": 2, "xt": 2, "qk": 4, "v": 2, "ft": 2, "ffn": 2},
}


def round_to_fp8(eng, z, magic, t, out, over, link):
    link(eng.tensor_scalar(magic.bitcast(I32), z.bitcast(I32), EXPONENT_BITS, None, ALU.bitwise_and))
    link(eng.tensor_scalar(magic, magic, FP8_MIN_NORMAL, FP8_MAGIC, ALU.max, ALU.mult))
    link(eng.tensor_tensor(t, z, magic, ALU.add))
    link(eng.tensor_tensor(out, t, magic, ALU.subtract))
    link(eng.tensor_scalar(over, out, FP8_OVERFLOW, 0.0, ALU.mult, ALU.mult))
    link(eng.tensor_tensor(out, out, over, ALU.add))


def layer(nc, L, x_in, x_out, w, consts):
    NB, S, D = x_in.shape
    NT = S // P
    KT = D // P
    NQUAD = HEADS // QUAD
    CAUSAL = L == 1
    ALIBI = 3 if CAUSAL else 0
    KA = QK_ROWS + ALIBI
    KB = KA + M_ROWS
    NQK = PER[L]["qk"]
    NVT = PER[L]["v"]
    KHEADS = 2 * HEADS if CAUSAL else 2
    UNIT_LOADS = 2 * len(Q_PARTS)
    FULL = NT * BANK
    EXP_BANKS, MAX_BANKS = BANKS[L]

    x_tiles = x_in.rearrange("b (t p) d -> b p t d", p=P)
    out_tiles = x_out.rearrange("b (t p) d -> b p t d", p=P)
    per = PER[L]
    tasks = TASKS[L]
    flat = [(s, *t) for s in range(HEADS) for t in tasks[s]]

    def valid(c):
        return not isinstance(c, int) or 0 <= c < NB

    def due(value):
        return not isinstance(value, int) or value > 0

    def over_bodies(eng, body):
        for b in range(-2, 4):
            body(b, b % 2)
        with eng.Fori(2, NB // 2 - 1) as i:
            body(i * 2, 0)
            body(i * 2 + 1, 1)
        for b in range(NB - 2, NB + 2):
            body(b, b % 2)

    def span(T):
        return (P * T, S - P * T) if CAUSAL else (0, S)

    def p_at(j, T):
        if not CAUSAL:
            return j * FULL + T * BANK
        pair = (j // 2) * (FULL + BANK)
        return pair + (T * BANK if j % 2 == 0 else FULL - (BANK - P) * T)

    P_COLS = 2 * (FULL + BANK) if CAUSAL else QUAD * FULL

    with ExitStack() as ctx:
        def sb(name, shape, dt):
            return ctx.enter_context(nc.sbuf_tensor(f"{name}_{L}", shape, dt))

        def sem(name):
            return ctx.enter_context(nc.semaphore(f"{name}_{L}"))

        qk_dram = nc.dram_tensor(f"qk_parts_{L}", [2, 3, NQK, P, S], BF16).ap()

        ident = sb("ident", [P, P], F32)
        identb = sb("identb", [P, P], BF16)
        maskb = sb("maskb", [P, P], BF16)
        w_qk = sb("w_qk", [P, KT, NQK * P], F32)
        w_v = sb("w_v", [P, KT, D if CAUSAL else 2 * DH], F32)
        w_o = sb("w_o", [P, KT, D], F32)
        xin = sb("xin", [P, 2, NT, D], F32)
        xres = sb("xres", [P, 2, NT, D], F32)
        stats = sb("stats", [P, 2, NT, 6], F32)
        meanvar = sb("meanvar", [P, 2, NT, 2], F32)
        neg_mean = sb("neg_mean", [P, 2, NT], F32)
        var_eps = sb("var_eps", [P, 2, NT], F32)
        rstd = sb("rstd", [P, 2, NT], F32)
        minus_half = sb("minus_half", [P, NT], F32)
        xT = sb("xT", [P, 2, KT, S], F32)
        qf = sb("qf", [P, 2, S], F32)
        qr = sb("qr", [P, S], F32)
        qparts = sb("qparts", [P, 2, 3, S], BF16)
        q_op = sb("q_op", [KB, 2 * HEADS, S], BF16)
        k_op = sb("k_op", [KB, KHEADS, S], BF16)
        v_op = sb("v_op", [P, 2, NT, HEADS if CAUSAL else 1, VW], F32)
        maxima = sb("maxima", [P, 2, NT, QUAD], F32)
        if CAUSAL:
            mask = sb("mask", [P, P], F32)
            max_before = sb("max_before", [P, 2, NT - 1, QUAD], F32)
        mparts = sb("mparts", [P, 2, NT, M_ROWS, QUAD], BF16)
        mrows = sb("mrows", [M_ROWS * QUAD, 2, S], BF16)
        probs = sb("probs", [P, 2, P_COLS], F32)
        oT = sb("oT", [P, 2, S], F32)
        recip = sb("recip", [P, 2, NT, QUAD], F32)
        o_rows = sb("o_rows", [P, 2, NT, D], F32)
        o_cols = sb("o_cols", [P, KT, S], F32)
        x1 = sb("x1", [P, 2, NT, D], F32)
        xo = sb("xo", [P, 2, NT, D], F32)
        if CAUSAL:
            xn2 = sb("xn2", [P, NT, D], F32)
            fT = o_cols
            w_f = sb("w_f", [P, KT, D], F32)
            bias = sb("bias", [P, D], F32)
            spare = xo[:, :, :, :].rearrange("p b t d -> p (b t d)")
            lora_down, lora_up = spare[0:100, 0:4], spare[0:4, 8:58]
            down_aux, up_aux = spare[0:100, D:2 * D], spare[0:50, 2 * D:3 * D]
            lora1, lora2 = spare[0:4, 3 * D:4 * D], spare[0:50, 4 * D:5 * D]
        else:
            kvf = sb("kvf", [2 * DH, 2, S], F32)
            kr = sb("kr", [2 * DH, S], F32)
            kparts = sb("kparts", [2 * DH, 2, 3, S], BF16)
            xn2 = sb("xn2", [P, NT, D], BF16)
            z8 = sb("z8", [P, NT, D], F32)
            magic8 = sb("magic8", [P, NT, D], F32)
            xq = sb("xq", [P, NT, D], BF16)
            fT = sb("fT", [P, KT, S], BF16)
            kern = sb("kern", [P, KT, D], BF16)
            w_f = sb("w_f", [P, KT, D], BF16)
            bias = sb("bias", [P, D], BF16)
            scales = sb("scales", [P, 3], F32)
            inverse = sb("inverse", [P, 2], F32)
            s_prod = sb("s_prod", [P, 1], F32)
            y = sb("y", [P, 2, 2, D], BF16)
            yb = sb("yb", [P, 2, 2, D], BF16)

        ps_exp = ctx.enter_context(nc.psum_tensor(f"ps_exp_{L}", [P, EXP_BANKS, BANK], F32))
        ps_max = ctx.enter_context(nc.psum_tensor(f"ps_max_{L}", [P, MAX_BANKS, BANK], F32))
        ps_pv = ctx.enter_context(nc.psum_tensor(f"ps_pv_{L}", [P, BANK], F32))
        ps_task = ctx.enter_context(nc.psum_tensor(f"ps_task_{L}", [P, 2, BANK], F32))

        consts_in = sem("consts_in")
        ready0 = sem("ready0")
        prep = sem("prep")
        prep_pe = sem("prep_pe")
        prep_act = sem("prep_act")
        x_loaded = [sem("x_loaded_0"), sem("x_loaded_1")]
        xres_loaded = [sem("xres_loaded_0"), sem("xres_loaded_1")]
        stats_done = [sem("stats1"), sem("stats2")]
        meanvar_ready = [sem("meanvar1"), sem("meanvar2")]
        ln_step = [sem("ln1_step"), sem("ln2_step")]
        xn_ready = [sem("xn1_ready"), sem("xn2_ready")]
        split_step = sem("split_step")
        qk_split = sem("qk_split")
        kv_step = sem("kv_step")
        kv_split = sem("kv_split")
        qk_stored = [sem("qk_stored_0"), sem("qk_stored_1")]
        op_loaded = [sem("op_loaded_0"), sem("op_loaded_1")]
        max_full = sem("max_full")
        max_done = sem("max_done")
        m_step = sem("m_step")
        m_split = sem("m_split")
        m_loaded = sem("m_loaded")
        exp_full = sem("exp_full")
        exp_done = sem("exp_done")
        pv_done = sem("pv_done")
        pv_copied = sem("pv_copied")
        rec_done = sem("rec_done")
        z_ready = sem("z_ready")
        magic_step = sem("magic_step")
        magic_ready = sem("magic_ready")
        fp8_step = sem("fp8_step")
        ffn_in = sem("ffn_in")
        yb_ready = sem("yb_ready")
        x1b_ready = sem("x1b_ready")
        stored = [sem("stored_0"), sem("stored_1")]
        ps_full = {k: sem(f"{k}_full") for k in per}
        ps_out = {k: sem(f"{k}_out") for k in per}
        o_ready = ps_out["ffn"] if CAUSAL else sem("o_ready")
        N_CONSTS = 16 * len(consts)

        def every_other(c, par):
            return 8 * (c - par) + 16

        def count(kind, c, k):
            return c * per[kind] + k + 1

        def bank_of(n, b, par):
            return (par * len(flat) + n) % 2

        def by_vector(kind):
            return kind in ("otr", "out") or (kind == "ffn" and CAUSAL)

        def last_in_bank(n, b, par):
            m, c = n - 2, b
            while True:
                while m < 0:
                    m, c = m + len(flat), c - 1
                _, kind, k, d = flat[m]
                if isinstance(c, int) and c < -2:
                    return None
                if valid(c + d):
                    return ps_out[kind], count(kind, c + d, k)
                m -= 2

        def tile_bank(banks, par, n):
            at = par * HEADS * NT + n
            last = max(m for m in range(at - 2 * HEADS * NT, at) if m % (2 * HEADS * NT) % banks == at % banks)
            return at % banks, at - last

        def left_before(s, b, par):
            if s == 0:
                b, par = b - 1, 1 - par
            if isinstance(b, int) and b < -2:
                return []
            return [(n, b, par) for n in range(len(flat)) if flat[n][0] == (s - 1) % HEADS]

        def a_head(s, b, par):
            return (b, par, s + 2 * QUAD) if s < HEADS - 2 * QUAD else (b + 1, 1 - par, s - (HEADS - 2 * QUAD))

        def pv_quad(s, b, par):
            return (b - 1, 1 - par, NQUAD - 1) if s < QUAD else (b, par, s // QUAD - 1)

        block = ctx.enter_context(nc.Block())

        @block.sync
        def _(sp):
            places = {
                "ident": ident[:, :], "identb": identb[:, :], "maskb": maskb[:, :],
                "w_qk": w_qk[:, :, :], "w_v": w_v[:, :, :], "w_o": w_o[:, :, :], "bias": bias[:, :],
                "k_aux": k_op[QK_ROWS:KB, :, :],
            }
            if CAUSAL:
                places |= {"mask": mask[:, :], "q_aux0": q_op[QK_ROWS:KA, 0:HEADS, :], "q_aux1": q_op[QK_ROWS:KA, HEADS:, :],
                           "w_f": w_f[:, :, :], "lora_down": lora_down, "down_aux": down_aux,
                           "lora_up": lora_up, "up_aux": up_aux}
            else:
                places |= {"kern": kern[:, :, :], "scale": scales[:, 0:1], "s_in": scales[:, 1:2],
                           "s_k": scales[:, 2:3]}
            for name, ap in consts.items():
                sp.dma_start(places[name], ap).then_inc(consts_in, 16)

            def load_x(c, par):
                if not valid(c):
                    return
                if due(seen := (c - 2) * per["xt"] + 2):
                    sp.wait_ge(ps_full["xt"], seen)
                sp.dma_start(xin[:, par, :, :], x_tiles[c]).then_inc(x_loaded[par], 16)

            def load_residual(c, par):
                if not valid(c):
                    return
                if CAUSAL:
                    if due(seen := 2 * (c - 1)):
                        sp.wait_ge(o_ready, seen)
                else:
                    if due(seen := 2 * (c - 1)):
                        sp.wait_ge(ps_out["out"], seen)
                sp.dma_start(xres[:, par, :, :], x_tiles[c]).then_inc(xres_loaded[par], 16)

            def load_maxima(c, par, quad):
                if not valid(c):
                    return
                n = c * NQUAD + quad
                sp.wait_ge(ps_out["m"], n + 1)
                first = par * HEADS + quad * QUAD
                for r in range(M_ROWS):
                    sp.dma_start(q_op[KA + r:KA + r + 1, first:first + QUAD, :],
                                 mrows[r * QUAD:(r + 1) * QUAD, quad % 2, :]).then_inc(m_loaded, 16)

            def store_parts(c, par, k):
                if not valid(c):
                    return
                for unit in range(2):
                    loads = (2 if CAUSAL or unit == 0 else 1) * len(Q_PARTS)
                    if due(seen := 16 * loads * (c - 1)):
                        sp.wait_ge(op_loaded[unit], seen)
                sp.wait_ge(qk_split, c * NQK + k + 1)
                sp.dma_start(qk_dram[par, :, k, :, :].rearrange("a p s -> p a s"),
                             qparts[:, k % 2, :, :]).then_inc(qk_stored[k % 2], 16)

            def load_operands(c, par, unit):
                if not valid(c):
                    return
                if CAUSAL:
                    for k in range(2):
                        sp.wait_ge(qk_stored[k], 16 * (2 * c + unit + 1))
                else:
                    sp.wait_ge(qk_stored[unit], 16 * (c + 1))
                if due(seen := (c - 1) * HEADS * NT):
                    sp.wait_ge(exp_full, seen)
                h0 = par * HEADS + unit * 8
                for g in range(len(Q_PARTS)):
                    rows = slice(g * DH, (g + 1) * DH)
                    src = qk_dram[par, Q_PARTS[g], 2 * unit if CAUSAL else unit, :, :]
                    sp.dma_start(q_op[rows, h0:h0 + 8, :],
                                 src.rearrange("(h d) s -> d h s", d=DH)).then_inc(op_loaded[unit], 16)
                    if CAUSAL:
                        src = qk_dram[par, K_PARTS[g], 2 * unit + 1, :, :]
                        sp.dma_start(k_op[rows, h0:h0 + 8, :],
                                     src.rearrange("(h d) s -> d h s", d=DH)).then_inc(op_loaded[unit], 16)
                    elif unit == 0:
                        if g == 0:
                            sp.wait_ge(kv_split, c + 1)
                        sp.dma_start(k_op[rows, par, :],
                                     kparts[0:DH, par, K_PARTS[g], :]).then_inc(op_loaded[unit], 16)

            def store_out(c, par):
                if not valid(c):
                    return
                sp.wait_ge(o_ready, 2 * c + 2)
                sp.dma_start(out_tiles[c], xo[:, par, :, :]).then_inc(stored[par], 16)

            def body(b, par):
                load_x(b + 2, par)
                load_residual(b - 1, 1 - par)
                load_maxima(b, par, 1)
                if CAUSAL:
                    store_parts(b + 1, 1 - par, 2)
                    load_operands(b + 1, 1 - par, 0)
                    store_parts(b + 1, 1 - par, 3)
                    load_operands(b + 1, 1 - par, 1)
                else:
                    store_parts(b + 1, 1 - par, 0)
                    load_operands(b + 1, 1 - par, 0)
                    store_parts(b + 1, 1 - par, 1)
                load_maxima(b, par, 2)
                if not CAUSAL:
                    load_operands(b + 1, 1 - par, 1)
                store_out(b - 2, par)
                load_maxima(b, par, 3)
                load_maxima(b + 1, 1 - par, 0)
                if CAUSAL:
                    store_parts(b + 2, par, 0)
                    store_parts(b + 2, par, 1)

            over_bodies(sp, body)
            for par in range(2):
                sp.wait_ge(stored[par], 8 * NB)

        @block.tensor
        def _(pe):
            pe.wait_ge(consts_in, N_CONSTS)
            if CAUSAL:
                pe.matmul(ps_task[0:4, 0, 0:D], lora_down[:, :], down_aux[:, :],
                          start=True, stop=True).then_inc(prep_pe, 1)
                pe.wait_ge(prep_act, 1)
                pe.matmul(ps_task[0:50, 1, 0:D], lora_up[:, :], lora1[:, :],
                          start=True, stop=True).then_inc(prep_pe, 1)
                pe.wait_ge(prep_act, 2)
                for kt in range(KT):
                    mm = pe.matmul(ps_task[:, 0, kt * D:(kt + 1) * D], lora2[:, kt * P:(kt + 1) * P],
                                   up_aux[:, :], start=True, stop=True)
                mm.then_inc(prep_pe, 1)
            pe.wait_ge(ready0, 2)

            def max_tile(s, b, par, i):
                c, cp, h = a_head(s, b, par)
                if not valid(c):
                    return
                n = HEADS * NT * c + NT * h + i
                if i == 0 and h % 8 == 0:
                    pe.wait_ge(op_loaded[h // 8], 16 * (UNIT_LOADS if CAUSAL or h < 8 else len(Q_PARTS)) * (c + 1))
                bank, ago = tile_bank(MAX_BANKS, cp, NT * h + i)
                if due(seen := n - ago + 1):
                    pe.wait_ge(max_done, seen)
                keys = (i + 1) * P if CAUSAL else S
                kh = cp * HEADS + h if CAUSAL else cp
                pe.matmul(ps_max[:, bank, 0:keys], q_op[0:KA, cp * HEADS + h, i * P:(i + 1) * P],
                          k_op[0:KA, kh, 0:keys], start=True, stop=True).then_inc(max_full, 1)

            def exp_tile(s, b, par, T):
                if not valid(b):
                    return
                n = HEADS * NT * b + NT * s + T
                bank, ago = tile_bank(EXP_BANKS, par, NT * s + T)
                if T == 0 and s % QUAD == 0:
                    pe.wait_ge(m_loaded, 16 * M_ROWS * (b * NQUAD + s // QUAD + 1))
                if due(seen := n - ago + 1):
                    pe.wait_ge(exp_done, seen)
                q0, nq = span(T)
                kh = par * HEADS + s if CAUSAL else par
                mm = pe.matmul(ps_exp[:, bank, 0:nq], k_op[0:KB, kh, T * P:(T + 1) * P],
                               q_op[0:KB, par * HEADS + s, q0:q0 + nq], start=True, stop=not CAUSAL)
                if CAUSAL:
                    mm = pe.matmul(ps_exp[:, bank, 0:P], maskb[:, :], identb[:, :], start=False, stop=True)
                mm.then_inc(exp_full, 1)

            def pv_tile(s, b, par):
                c, cp, quad = pv_quad(s, b, par)
                if not valid(c):
                    return
                T, n = s % QUAD, NQUAD * c + quad
                if T == 0:
                    if quad == 0:
                        pe.wait_ge(ps_out["v"], per["v"] * (c + 1))
                    pe.wait_ge(exp_done, NT * QUAD * (n + 1))
                    if due(seen := n):
                        pe.wait_ge(pv_copied, seen)
                q0, nq = span(T)
                for j in range(QUAD):
                    at = p_at(j, T)
                    mm = pe.matmul(ps_pv[VW * j:VW * (j + 1), q0:q0 + nq],
                                   v_op[:, cp, T, quad * QUAD + j if CAUSAL else 0, :],
                                   probs[:, quad % 2, at:at + nq],
                                   start=(T == 0), stop=(T == NT - 1))
                if T == NT - 1:
                    mm.then_inc(pv_done, 1)

            def task(n, b, par):
                _, kind, k, d = flat[n]
                c = b + d
                if not valid(c):
                    return
                cp = (par + d) % 2
                ps = ps_task[:, bank_of(n, b, par), :]
                half = ps.bitcast(BF16)
                if last := last_in_bank(n, b, par):
                    pe.wait_ge(*last)
                if kind == "m":
                    pe.wait_ge(m_split, c * NQUAD + k + 1)
                    for t in range(NT):
                        mm = pe.transpose(half[0:M_ROWS * QUAD, t * P:(t + 1) * P],
                                          mparts[:, k % 2, t, :, :].rearrange("p r j -> p (r j)"), identb[:, :])
                elif kind == "otr":
                    pe.wait_ge(pv_copied, c * NQUAD + k + 1)
                    for t in range(NT):
                        mm = pe.transpose(ps[:, t * P:(t + 1) * P], oT[:, k % 2, t * P:(t + 1) * P], ident[:, :])
                elif kind == "ont":
                    pe.wait_ge(ps_out["otr"], c * NQUAD + 2 * k + 2)
                    for t in range(NT):
                        mm = pe.transpose(ps[:, t * P:(t + 1) * P], o_rows[:, cp, t, k * P:(k + 1) * P], ident[:, :])
                elif kind == "xt":
                    pe.wait_ge(xn_ready[0], NT * (c + 1))
                    for t in range(NT):
                        mm = pe.transpose(ps[:, t * P:(t + 1) * P], xin[:, cp, t, k * P:(k + 1) * P], ident[:, :])
                elif kind == "qk":
                    pe.wait_ge(ps_out["xt"], per["xt"] * (c + 1))
                    for kt in range(KT):
                        mm = pe.matmul(ps[:, :], w_qk[:, kt, k * P:(k + 1) * P], xT[:, cp, kt, :],
                                       start=(kt == 0), stop=(kt == KT - 1))
                elif kind == "kv":
                    pe.wait_ge(ps_out["xt"], per["xt"] * (c + 1))
                    for kt in range(KT):
                        mm = pe.matmul(ps[0:2 * DH, :], w_v[:, kt, :], xT[:, cp, kt, :],
                                       start=(kt == 0), stop=(kt == KT - 1))
                elif kind == "v" and CAUSAL:
                    pe.wait_ge(ps_out["xt"], per["xt"] * (c + 1))
                    for t in (2 * k, 2 * k + 1):
                        for kt in range(KT):
                            mm = pe.matmul(ps[:, (t % 2) * D:(t % 2 + 1) * D], xT[:, cp, kt, t * P:(t + 1) * P],
                                           w_v[:, kt, :], start=(kt == 0), stop=(kt == KT - 1))
                elif kind == "v":
                    pe.wait_ge(ps_out["kv"], c + 1)
                    pe.nop(nofuse=True)
                    for t in range(NT):
                        mm = pe.transpose(ps[:, t * 2 * DH:(t + 1) * 2 * DH], kvf[:, cp, t * P:(t + 1) * P],
                                          ident[0:2 * DH, 0:2 * DH])
                elif kind == "out":
                    pe.wait_ge(ps_out["ont"], per["ont"] * (c + 1))
                    for t in (2 * k, 2 * k + 1):
                        for kt in range(KT):
                            mm = pe.matmul(ps[:, (t % 2) * D:(t % 2 + 1) * D], o_cols[:, kt, t * P:(t + 1) * P],
                                           w_o[:, kt, :], start=(kt == 0), stop=(kt == KT - 1))
                elif kind == "ft" and CAUSAL:
                    pe.wait_ge(xn_ready[1], NT * (c + 1))
                    for t in range(NT):
                        mm = pe.transpose(ps[:, t * P:(t + 1) * P], xn2[:, t, k * P:(k + 1) * P], ident[:, :])
                elif kind == "ft":
                    pe.wait_ge(ffn_in, c + 1)
                    for kt in range(KT):
                        for t in range(NT):
                            mm = pe.transpose(half[:, kt * S + t * P:kt * S + (t + 1) * P],
                                              xq[:, t, kt * P:(kt + 1) * P], identb[:, :])
                elif kind == "ffn":
                    pe.wait_ge(ps_out["ft"], per["ft"] * (c + 1))
                    for t in (2 * k, 2 * k + 1):
                        for kt in range(KT):
                            mm = pe.matmul(ps[:, (t % 2) * D:(t % 2 + 1) * D], fT[:, kt, t * P:(t + 1) * P],
                                           w_f[:, kt, :], start=(kt == 0), stop=(kt == KT - 1))
                mm.then_inc(ps_full[kind], 1)

            def body(b, par):
                n = 0
                for s in range(HEADS):
                    for step in ORDER[L].split():
                        if step == "E3" and s % QUAD == 0:
                            task(n, b, par)
                            n += 1
                        if step[0] == "A":
                            max_tile(s, b, par, int(step[1]))
                        elif step[0] == "E":
                            exp_tile(s, b, par, int(step[1]))
                        else:
                            pv_tile(s, b, par)
                    while n < len(flat) and flat[n][0] == s:
                        task(n, b, par)
                        n += 1

            over_bodies(pe, body)

        @block.scalar
        def _(act):
            if CAUSAL:
                act.wait_ge(prep_pe, 1)
                act.activation(lora1[:, :], ps_task[0:4, 0, 0:D], ACT.Copy).then_inc(prep_act, 1)
                act.wait_ge(prep_pe, 2)
                act.activation(lora2[:, :], ps_task[0:50, 1, 0:D], ACT.Copy).then_inc(prep_act, 1)
            act.wait_ge(ready0, 2)

            def exp_tile(s, b, par, T):
                if not valid(b):
                    return
                n = HEADS * NT * b + NT * s + T
                bank, _ = tile_bank(EXP_BANKS, par, NT * s + T)
                quad = s // QUAD
                if s % QUAD == 0 and T == 0:
                    if due(seen := NQUAD * b + quad - 1):
                        act.wait_ge(pv_done, seen)
                act.wait_ge(exp_full, n + 1)
                _, nq = span(T)
                at = p_at(s % QUAD, T)
                act.activation(probs[:, quad % 2, at:at + nq], ps_exp[:, bank, 0:nq], ACT.Exp).then_inc(exp_done, 1)

            def copy_pv(s, b, par):
                c, _, quad = pv_quad(s, b, par)
                if not valid(c):
                    return
                n = NQUAD * c + quad
                if due(seen := n - 1):
                    act.wait_ge(ps_full["otr"], seen)
                act.wait_ge(pv_done, n + 1)
                act.activation(oT[:, quad % 2, :], ps_pv[:, :], ACT.Copy).then_inc(pv_copied, 1)

            def copy_task(n, b, par):
                _, kind, k, d = flat[n]
                c = b + d
                if not valid(c) or by_vector(kind):
                    return
                cp = (par + d) % 2
                ps = ps_task[:, bank_of(n, b, par), :]
                half = ps.bitcast(BF16)
                if kind == "m":
                    if due(seen := 16 * M_ROWS * (c * NQUAD + k - 1)):
                        act.wait_ge(m_loaded, seen)
                    dst, src = mrows[:, k % 2, :], half[0:M_ROWS * QUAD, 0:S]
                elif kind == "ont":
                    last = "ffn" if CAUSAL else "out"
                    if due(seen := per[last] * c):
                        act.wait_ge(ps_full[last], seen)
                    dst, src = o_cols[:, k, :], ps
                elif kind == "xt":
                    dst, src = xT[:, cp, k, :], ps
                elif kind == "qk":
                    if due(seen := NQK * c + k - 1):
                        act.wait_ge(qk_split, seen)
                    dst, src = qf[:, k % 2, :], ps
                elif kind == "kv":
                    if due(seen := c - 1):
                        act.wait_ge(kv_split, seen)
                    dst, src = kvf[:, cp, :], ps[0:2 * DH, :]
                elif kind == "v" and CAUSAL:
                    dst = v_op[:, cp, 2 * k:2 * k + 2, :, 0:DH]
                    src = ps.rearrange("p (t h d) -> p t h d", t=2, d=DH)
                elif kind == "v":
                    dst = v_op[:, cp, :, 0, 0:DH]
                    src = ps[:, 0:NT * 2 * DH].rearrange("p (t a d) -> p t a d", a=2, d=DH)[:, :, 1, :]
                elif kind == "ft":
                    if CAUSAL:
                        act.wait_ge(ps_full["out"], per["out"] * (c + 1))
                    else:
                        if due(seen := per["ffn"] * c):
                            act.wait_ge(ps_full["ffn"], seen)
                    if CAUSAL:
                        dst, src = fT[:, k, :], ps
                    else:
                        dst, src = fT[:, :, :].rearrange("p k s -> p (k s)"), half
                elif kind == "ffn":
                    if due(seen := 2 * c + k - 1):
                        act.wait_ge(yb_ready, seen)
                    dst, src = y[:, k, :, :].rearrange("p t d -> p (t d)"), ps
                act.wait_ge(ps_full[kind], count(kind, c, k))
                if kind == "qk" and not CAUSAL:
                    ins = act.activation(dst, src, ACT.Identity, scale=scales[:, 0:1])
                elif kind == "qk" and k % 2 == 0:
                    ins = act.activation(dst, src, ACT.Copy, scale=float(DH) ** -0.5)
                elif kind == "ffn":
                    ins = act.activation(dst, src, ACT.Identity, scale=s_prod[:, 0:1])
                else:
                    ins = act.activation(dst, src, ACT.Copy)
                ins.then_inc(ps_out[kind], 1)

            def body(b, par):
                for s in range(HEADS):
                    exp_tile(s, b, par, 0)
                    exp_tile(s, b, par, 1)
                    for n, bb, pp in left_before(s, b, par):
                        if flat[n][1] != "m":
                            copy_task(n, bb, pp)
                    exp_tile(s, b, par, 2)
                    exp_tile(s, b, par, 3)
                    if s % QUAD == 0:
                        copy_task([t[:2] for t in flat].index((s, "m")), b, par)
                    if s % QUAD == QUAD - 1:
                        copy_pv(s, b, par)

            over_bodies(act, body)

        @block.vector
        def _(dve):
            steps = [0]

            def link(ins):
                steps[0] += 1
                ins.then_inc(prep, 1)
                dve.wait_ge(prep, steps[0])

            link(dve.memset(v_op[:, :, :, :, :].rearrange("p b t h v -> p (b t h v)"), 0.0))
            for par in range(2):
                link(dve.memset(v_op[:, par, :, :, DH:DH + 1], 1.0))
            dve.wait_ge(consts_in, N_CONSTS)
            if CAUSAL:
                dve.wait_ge(prep_pe, 3)
                link(dve.tensor_tensor(w_f[:, :, :].rearrange("p k d -> p (k d)"), ps_task[:, 0, 0:KT * D],
                                       w_f[:, :, :].rearrange("p k d -> p (k d)"), ALU.add))
            else:
                link(dve.reciprocal(inverse[:, :], scales[:, 1:3]))
                link(dve.tensor_tensor(s_prod[:, :], scales[:, 1:2], scales[:, 2:3], ALU.mult))
                link(dve.tensor_scalar(z8[:, 0:KT, :], kern[:, :, :], inverse[:, 1:2], None, ALU.mult))
                round_to_fp8(dve, z8[:, 0:KT, :], magic8[:, 0:KT, :], z8[:, KT:2 * KT, :],
                             w_f[:, :, :], xn2[:, 0:KT, :], link)
            dve.memset(minus_half[:, :], -0.5).then_inc(ready0, 2)

            def max_tile(s, b, par, i):
                c, cp, h = a_head(s, b, par)
                if not valid(c):
                    return
                bank, _ = tile_bank(MAX_BANKS, cp, NT * h + i)
                dve.wait_ge(max_full, HEADS * NT * c + NT * h + i + 1)
                at = maxima[:, (h // QUAD) % 2, i, h % QUAD:h % QUAD + 1]
                if CAUSAL:
                    if i > 0:
                        before = max_before[:, (h // QUAD) % 2, i - 1, h % QUAD:h % QUAD + 1]
                        dve.tensor_reduce(before, ps_max[:, bank, 0:i * P], AX.X, ALU.max)
                    else:
                        dve.nop(nofuse=True)
                    block = ps_max[:, bank, i * P:(i + 1) * P]
                    ins = dve.tensor_tensor_reduce(block, block, mask[:, :], 1.0, LOWEST, ALU.add, ALU.max, at)
                else:
                    ins = dve.tensor_reduce(at, ps_max[:, bank, :], AX.X, ALU.max)
                ins.then_inc(max_done, 1)

            def split_maxima(s, b, par):
                c, _, h = a_head(s, b, par)
                if not valid(c):
                    return
                quad = h // QUAD
                n = c * NQUAD + quad
                dve.wait_ge(max_done, NT * QUAD * (n + 1))
                if due(seen := n - 1):
                    dve.wait_ge(ps_full["m"], seen)
                hi, lo = mparts[:, quad % 2, :, 0, :], mparts[:, quad % 2, :, 1, :]
                m = maxima[:, quad % 2, :, :]
                if CAUSAL:
                    dve.tensor_tensor(m[:, 1:NT, :], m[:, 1:NT, :], max_before[:, quad % 2, :, :],
                                      ALU.max).then_inc(m_step, 1)
                    dve.wait_ge(m_step, 2 * n + 1)
                dve.tensor_scalar(hi, m, -1.0, None, ALU.mult).then_inc(m_step, 1)
                dve.wait_ge(m_step, (2 if CAUSAL else 1) * (n + 1))
                dve.scalar_tensor_tensor(lo, m, -1.0, hi, ALU.mult, ALU.subtract).then_inc(m_split, 1)

            def statistics(which, c, cp, t):
                if not valid(c):
                    return
                src = x1 if which else xin
                if t == 0:
                    if which:
                        dve.wait_ge(ps_out["out"], 2 * c + 2)
                    else:
                        dve.wait_ge(x_loaded[cp], every_other(c, cp))
                    if due(seen := NT * c):
                        dve.wait_ge(meanvar_ready[which], seen)
                        dve.wait_ge(xn_ready[which], seen)
                dve.bn_stats(stats[:, which, t, :], src[:, cp, t, :]).then_inc(stats_done[which], 1)
                if t == NT - 1:
                    dve.wait_ge(stats_done[which], NT * (c + 1))
                    dve.nop(nofuse=True)
                    for t in range(NT):
                        dve.bn_aggr(meanvar[:, which, t, :], stats[:, which, t, :]).then_inc(meanvar_ready[which], 1)

            def magic(c, half, step):
                if not valid(c):
                    return
                tiles = slice(2 * half, 2 * half + 2)
                z, m = z8[:, tiles, :], magic8[:, tiles, :]
                if step == 0:
                    dve.wait_ge(z_ready, c + 1)
                    if due(seen := c):
                        dve.wait_ge(ffn_in, seen)
                    dve.tensor_scalar(m.bitcast(I32), z.bitcast(I32), EXPONENT_BITS, None,
                                      ALU.bitwise_and).then_inc(magic_step, 1)
                else:
                    dve.wait_ge(magic_step, 2 * c + half + 1)
                    dve.tensor_scalar(m, m, FP8_MIN_NORMAL, FP8_MAGIC, ALU.max, ALU.mult).then_inc(magic_ready, 1)

            def take_task(n, b, par):
                _, kind, k, d = flat[n]
                c = b + d
                if not valid(c):
                    return
                cp = (par + d) % 2
                ps = ps_task[:, bank_of(n, b, par), :]
                dve.wait_ge(ps_full[kind], count(kind, c, k))
                if kind == "otr":
                    heads = ps.rearrange("p (t j v) -> p t j v", t=NT, j=QUAD)
                    dve.reciprocal(recip[:, k % 2, :, :], heads[:, :, :, DH]).then_inc(rec_done, 1)
                    dve.wait_ge(rec_done, c * NQUAD + k + 1)
                    if k == 0:
                        if due(seen := (c - 1) * per["ont"]):
                            dve.wait_ge(ps_full["ont"], seen)
                    dst = o_rows[:, cp, :, k * QUAD * DH:(k + 1) * QUAD * DH]
                    dve.tensor_tensor(dst.rearrange("p t (j d) -> p t j d", j=QUAD), heads[:, :, :, 0:DH],
                                      recip[:, k % 2, :, :].unsqueeze(3).to_broadcast([P, NT, QUAD, DH]),
                                      ALU.mult).then_inc(ps_out[kind], 1)
                elif kind == "out":
                    dve.wait_ge(xres_loaded[cp], every_other(c, cp))
                    if due(seen := 2 * (c - 1)):
                        dve.wait_ge(o_ready, seen)
                    flat2 = "p t d -> p (t d)"
                    dve.tensor_tensor(x1[:, cp, 2 * k:2 * k + 2, :].rearrange(flat2), ps,
                                      xres[:, cp, 2 * k:2 * k + 2, :].rearrange(flat2),
                                      ALU.add).then_inc(ps_out[kind], 1)
                else:
                    dve.wait_ge(x1b_ready, c + 1)
                    if due(seen := every_other(c - 2, cp)):
                        dve.wait_ge(stored[cp], seen)
                    flat2 = "p t d -> p (t d)"
                    dve.tensor_tensor(xo[:, cp, 2 * k:2 * k + 2, :].rearrange(flat2), ps,
                                      xres[:, cp, 2 * k:2 * k + 2, :].rearrange(flat2), ALU.add).then_inc(o_ready, 1)

            ahead = 2 if CAUSAL else 1

            def body(b, par):
                for s in range(HEADS):
                    max_tile(s, b, par, 0)
                    max_tile(s, b, par, 1)
                    before = [args for args in left_before(s, b, par) if by_vector(flat[args[0]][1])]
                    for args in before[:ahead]:
                        take_task(*args)
                    if s >= HEADS - 2 and not CAUSAL:
                        magic(b - 1, s - (HEADS - 2), 0)
                    max_tile(s, b, par, 2)
                    for args in before[ahead:]:
                        take_task(*args)
                    if s in (11, 12):
                        statistics(1, b - 1, 1 - par, 2 * (s - 11))
                    max_tile(s, b, par, 3)
                    if s in (11, 12):
                        statistics(1, b - 1, 1 - par, 2 * (s - 11) + 1)
                    if s % QUAD == QUAD - 1:
                        split_maxima(s, b, par)
                    if 1 <= s <= 4:
                        statistics(0, b + 2, par, s - 1)
                    if s >= HEADS - 2 and not CAUSAL:
                        magic(b - 1, s - (HEADS - 2), 1)

            over_bodies(dve, body)

        @block.gpsimd
        def _(pool):
            pool.wait_ge(ready0, 2)

            def settled():
                pool.nop(nofuse=True)

            def normalise(which, c, cp):
                if not valid(c):
                    return
                src = x1 if which else xin
                if which and CAUSAL:
                    if due(seen := per["ft"] * c):
                        pool.wait_ge(ps_full["ft"], seen)
                if which and not CAUSAL:
                    if due(seen := c):
                        pool.wait_ge(ffn_in, seen)
                pool.wait_ge(meanvar_ready[which], NT * (c + 1))
                settled()
                pool.tensor_scalar(neg_mean[:, which, :], meanvar[:, which, :, 0], -1.0, 0.0,
                                   ALU.mult, ALU.add).then_inc(ln_step[which], 1)
                pool.tensor_scalar(var_eps[:, which, :], meanvar[:, which, :, 1], 1.0, EPS,
                                   ALU.mult, ALU.add).then_inc(ln_step[which], 1)
                pool.wait_ge(ln_step[which], 3 * c + 2)
                pool.tensor_tensor(rstd[:, which, :], var_eps[:, which, :], minus_half[:, :],
                                   ALU.pow).then_inc(ln_step[which], 1)
                pool.wait_ge(ln_step[which], 3 * c + 3)
                settled()
                for t in range(NT):
                    dst = xn2[:, t, :] if which else xin[:, cp, t, :]
                    pool.tensor_scalar(dst, src[:, cp, t, :], neg_mean[:, which, t:t + 1],
                                       rstd[:, which, t:t + 1], ALU.add, ALU.mult).then_inc(xn_ready[which], 1)

            def split(src, parts, rest, step, at):
                settled()
                pool.tensor_scalar(parts[:, 0, :], src, 1.0, 0.0, ALU.mult, ALU.add).then_inc(step, 1)
                pool.wait_ge(step, at + 1)
                pool.tensor_tensor(rest, src, parts[:, 0, :], ALU.subtract).then_inc(step, 1)
                pool.wait_ge(step, at + 2)
                settled()
                pool.tensor_scalar(parts[:, 1, :], rest, 1.0, 0.0, ALU.mult, ALU.add).then_inc(step, 1)
                pool.wait_ge(step, at + 3)
                return pool.tensor_tensor(parts[:, 2, :], rest, parts[:, 1, :], ALU.subtract)

            def split_qk(c, k):
                if not valid(c):
                    return
                n = NQK * c + k
                if due(seen := n):
                    pool.wait_ge(qk_split, seen)
                if due(seen := 16 * ((2 if CAUSAL else 1) * c + k // 2)):
                    pool.wait_ge(qk_stored[k % 2], seen)
                pool.wait_ge(ps_out["qk"], n + 1)
                split(qf[:, k % 2, :], qparts[:, k % 2, :, :], qr[:, :], split_step, 3 * n).then_inc(qk_split, 1)

            def split_kv(c, cp):
                if not valid(c):
                    return
                if due(seen := c):
                    pool.wait_ge(kv_split, seen)
                if due(seen := 16 * UNIT_LOADS * (c - 1)):
                    pool.wait_ge(op_loaded[0], seen)
                pool.wait_ge(ps_out["kv"], c + 1)
                split(kvf[:, cp, :], kparts[:, cp, :, :], kr[:, :], kv_step, 3 * c).then_inc(kv_split, 1)

            def over_s_in(c):
                if not valid(c):
                    return
                pool.wait_ge(xn_ready[1], NT * (c + 1))
                settled()
                pool.tensor_scalar(z8[:, :, :], xn2[:, :, :], inverse[:, 0:1], 1.0,
                                   ALU.mult, ALU.mult).then_inc(z_ready, 1)

            def to_fp8(c):
                if not valid(c):
                    return
                pool.wait_ge(magic_ready, 2 * (c + 1))
                if due(seen := c):
                    pool.wait_ge(ps_full["ft"], seen)
                pool.tensor_tensor(z8[:, :, :], z8[:, :, :], magic8[:, :, :], ALU.add).then_inc(fp8_step, 1)
                pool.wait_ge(fp8_step, 3 * c + 1)
                pool.tensor_tensor(xq[:, :, :], z8[:, :, :], magic8[:, :, :], ALU.subtract).then_inc(fp8_step, 1)
                pool.wait_ge(fp8_step, 3 * c + 2)
                settled()
                pool.tensor_scalar(xn2[:, :, :], xq[:, :, :], FP8_OVERFLOW, 0.0,
                                   ALU.mult, ALU.mult).then_inc(fp8_step, 1)
                pool.wait_ge(fp8_step, 3 * c + 3)
                pool.tensor_tensor(xq[:, :, :], xq[:, :, :], xn2[:, :, :], ALU.add).then_inc(ffn_in, 1)

            def finish_ffn(c, cp, k):
                if not valid(c):
                    return
                pool.wait_ge(ps_out["ffn"], 2 * c + k + 1)
                pool.tensor_tensor(yb[:, k, :, :], y[:, k, :, :], bias[:, :].unsqueeze(1).to_broadcast([P, 2, D]),
                                   ALU.add).then_inc(yb_ready, 1)
                if due(seen := every_other(c - 2, cp)):
                    pool.wait_ge(stored[cp], seen)
                pool.wait_ge(yb_ready, 2 * c + k + 1)
                pool.tensor_tensor(xo[:, cp, 2 * k:2 * k + 2, :], x1[:, cp, 2 * k:2 * k + 2, :], yb[:, k, :, :],
                                   ALU.add).then_inc(o_ready, 1)

            def add_bias(c, cp):
                if not valid(c):
                    return
                pool.wait_ge(ps_out["out"], 2 * (c + 1))
                pool.tensor_tensor(xres[:, cp, :, :], x1[:, cp, :, :], bias[:, :].unsqueeze(1).to_broadcast([P, NT, D]),
                                   ALU.add).then_inc(x1b_ready, 1)

            def body_causal(b, par):
                split_qk(b + 1, 2)
                split_qk(b + 1, 3)
                add_bias(b - 2, par)
                normalise(0, b + 2, par)
                normalise(1, b - 1, 1 - par)
                split_qk(b + 2, 0)
                split_qk(b + 2, 1)

            def body_full(b, par):
                split_qk(b + 1, 1)
                normalise(0, b + 2, par)
                finish_ffn(b - 2, par, 0)
                finish_ffn(b - 2, par, 1)
                normalise(1, b - 1, 1 - par)
                over_s_in(b - 1)
                split_kv(b + 2, par)
                split_qk(b + 2, 0)
                to_fp8(b - 1)

            over_bodies(pool, body_causal if CAUSAL else body_full)


def build(nc, x, w, aux, out):
    D = x.shape[2]
    x_mid = nc.dram_tensor("x_mid", list(x.shape), F32).ap()

    def rows(ap):
        return ap.rearrange("(k p) n -> p k n", p=P)

    def spread(ap, n):
        return ap.unsqueeze(0).to_broadcast([P, n])

    S = x.shape[1]
    shared = {"ident": aux["ident"], "identb": aux["identb"], "maskb": aux["maskb"]}
    layer(nc, 0, x, x_mid, w, shared | {
        "w_qk": rows(w["wq0T"]), "w_v": rows(w["wkv0T"]), "w_o": rows(w["wo0T"]),
        "bias": spread(w["bias0"], D), "kern": rows(w["kernel0"]), "scale": spread(w["scale"], 1),
        "s_in": spread(w["s_in"], 1), "s_k": spread(w["s_k"], 1),
        "k_aux": aux["k_aux0"].unsqueeze(1).to_broadcast([M_ROWS, 2, S]),
    })
    layer(nc, 1, x_mid, out, w, shared | {
        "w_qk": rows(w["wqk1T"]), "w_v": rows(w["wv1T"]), "w_o": rows(w["wo1T"]),
        "bias": spread(w["b1"], D), "w_f": rows(w["W1T"]), "lora_down": w["lora_downT"],
        "down_aux": w["down_aux"], "lora_up": w["lora_upT"], "up_aux": w["up_auxT"],
        "k_aux": aux["k_aux1"].unsqueeze(1).to_broadcast([3 + M_ROWS, 2 * HEADS, S]),
        "mask": aux["mask"], "q_aux0": aux["q_aux1"], "q_aux1": aux["q_aux1"],
    })


def shape_constants(S, bf):
    import numpy as np
    eye = np.eye(P, dtype=np.float32)
    later = np.triu(np.ones((P, P), dtype=bool), 1)
    slopes = (2.0 ** (-8.0 / HEADS * (np.arange(HEADS) + 1.0))).astype(np.float32)
    q_aux = np.zeros((3, HEADS, S), dtype=bf)
    rest = slopes.copy()
    for r in range(3):
        part = rest.astype(bf)
        q_aux[r] = part[:, None]
        rest = rest - part.astype(np.float32)
    place = (np.arange(S) - S // 2).astype(bf)
    ones = np.ones((M_ROWS, S), dtype=bf)
    return {
        "ident": eye, "identb": eye.astype(bf),
        "mask": np.where(later, np.float32(-3e38), np.float32(0)),
        "maskb": np.where(later, np.float32(-3e38), np.float32(0)).astype(bf),
        "k_aux0": ones, "k_aux1": np.concatenate([np.stack([place] * 3), ones]), "q_aux1": q_aux,
    }


def kernel(**inputs):
    import numpy as np
    import concourse.bacc as bacc
    from concourse.bass_utils import run_bass_kernel_spmd

    a = {k: np.asarray(v) for k, v in inputs.items()}
    D = a["L0_attn_x"].shape[2]
    w_in = a["L1_attn_w_in"]
    half = P
    order = [w_in[0:half], w_in[D:D + half], w_in[half:D], w_in[D + half:2 * D]]
    w = {
        "wq0T": a["L0_attn_w_q"].T, "wkv0T": np.concatenate([a["L0_attn_w_k"], a["L0_attn_w_v"]]).T,
        "wo0T": a["L0_attn_w_out"].T, "kernel0": a["L0_ffn_kernel"], "bias0": a["L0_ffn_bias"],
        "scale": a["L0_attn_softmax_scale"], "s_in": a["L0_ffn_input_scale"], "s_k": a["L0_ffn_kernel_scale"],
        "wqk1T": np.concatenate(order).T, "wv1T": w_in[2 * D:3 * D].T, "wo1T": a["L1_attn_w_out"].T,
        "W1T": a["L1_ffn_W"].T, "b1": a["L1_ffn_b"], "lora_downT": a["L1_ffn_lora_down"].T,
        "lora_upT": a["L1_ffn_lora_up"].T, "down_aux": a["L1_ffn_down_aux"], "up_auxT": a["L1_ffn_up_aux"].T,
    }
    aux = shape_constants(a["L0_attn_x"].shape[1], a["L0_ffn_kernel"].dtype)

    nc = bacc.Bacc("TRN2", target_bir_lowering=False, num_devices=1)
    nc.disable_value_cache = True
    arrays = {}

    def declare(name, array):
        array = np.ascontiguousarray(array)
        arrays[f"in_{name}"] = array
        return nc.dram_tensor(f"in_{name}", array.shape, mybir.dt.from_np(array.dtype), kind="ExternalInput").ap()

    x = declare("x", a["L0_attn_x"])
    w = {k: declare(k, v) for k, v in w.items()}
    aux = {k: declare(k, v) for k, v in aux.items()}
    out = nc.dram_tensor("out", list(x.shape), F32, kind="ExternalOutput").ap()
    build(nc, x, w, aux, out)
    r = run_bass_kernel_spmd(nc, [arrays], core_ids=[0])
    return r.results[0]["out"]
```
